# Optimizing a Trainium2 kernel written in Bass

```python
import numpy as np
import jax
import jax.numpy as jnp

def _softmax(x, axis=-1):
    return jax.nn.softmax(x, axis=axis)

def _gelu(x):
    return jax.nn.gelu(x, approximate=True)

def _silu(x):
    return jax.nn.silu(x)

def _sigmoid(x):
    return jax.nn.sigmoid(x)

def _layernorm(x, axis=-1, eps=1e-05):
    m = jnp.mean(x, axis=axis, keepdims=True)
    v = jnp.var(x, axis=axis, keepdims=True)
    return (x - m) / jnp.sqrt(v + eps)

def _scatter_add(tgt, idx, src, axis=0):
    return tgt.at[idx].add(src)

def _segment_sum(src, seg, n):
    return jax.ops.segment_sum(src, seg, n)
kernel_name = 'mk_cond_resid_d1_seqx_r4_6f3255'

def setup_inputs(seed: int=0):
    np.random.seed(seed)
    _w = jnp.asarray

    def _rec_inputs():
        import jax
        import jax.numpy as jnp
        _rk = jax.random.key(seed)
        x = -0.0003929 + 0.9999 * jax.random.normal(jax.random.fold_in(_rk, 1), (128, 64, 256), jnp.float32)
        _lenS = 64 - jax.random.randint(jax.random.fold_in(_rk, 7), (128,), 0, max(1, 64 // 4) + 1, jnp.int32)
        _lenS2 = 64 - jax.random.randint(jax.random.fold_in(_rk, 8), (128,), 0, max(1, 64 // 4) + 1, jnp.int32)
        itok_B_0_63 = jax.random.randint(jax.random.fold_in(_rk, 11), (128,), 0, 64, jnp.int32)
        return (x, itok_B_0_63)
    x, itok_B_0_63 = _rec_inputs()

    def _L0_cond_setup():
        import jax, jax.numpy as jnp
        import numpy as np
        NUM_CATEGORIES = 64
        INPUT_DIM = 256
        HIDDEN_DIM = 256
        B = 64
        S = 64
        key = jax.random.key(seed)
        kx, kc, kw = jax.random.split(key, 3)
        x = jax.random.normal(kx, (B, S, INPUT_DIM), dtype=jnp.float32)
        cat_ids = jax.random.randint(kc, (B,), 0, NUM_CATEGORIES, dtype=jnp.int32)
        W = 0.02 * jax.random.normal(kw, (NUM_CATEGORIES, INPUT_DIM, HIDDEN_DIM), dtype=jnp.float32)
        b = jnp.zeros((NUM_CATEGORIES, HIDDEN_DIM), dtype=jnp.float32)
        return {'x': x, 'cat_ids': cat_ids, 'W': W, 'b': b}
    _L0_cond_all = _L0_cond_setup()
    _L0_cond_in = {k: v for k, v in _L0_cond_all.items() if k in ('W', 'b')}
    del _L0_cond_all
    return {'x': x, 'itok_B_0_63': itok_B_0_63, 'L0_cond_W': _L0_cond_in['W'], 'L0_cond_b': _L0_cond_in['b']}

def reference(x, itok_B_0_63, L0_cond_W, L0_cond_b):
    import jax
    import jax.numpy as jnp

    def _L0_cond_ref(x, cat_ids, W, b):
        import jax, jax.numpy as jnp
        import numpy as np
        NUM_CATEGORIES = 64
        INPUT_DIM = 256
        HIDDEN_DIM = 256
        B = 64
        S = 64
        selected_W = W[cat_ids]
        selected_b = b[cat_ids]
        out = jnp.einsum('bsd,bdh->bsh', x, selected_W) + selected_b[:, None, :]
        return out
    x = x + _L0_cond_ref(x, itok_B_0_63, L0_cond_W, L0_cond_b)
    return x

_drawn_inputs = setup_inputs


def setup_inputs(seed=0):
    import zlib

    import numpy as np

    out = dict(_drawn_inputs(seed))
    spreads = {'L0_cond_b': (0.0, 0.1)}
    factors = {}
    for name, (base, spread) in spreads.items():
        noise = np.random.default_rng([zlib.crc32(name.encode()), seed]).standard_normal(out[name].shape)
        drawn = base * np.exp(spread * noise) if base else spread * noise
        out[name] = jnp.asarray(drawn.astype(out[name].dtype))
    for name, factor in factors.items():
        out[name] = (out[name] * factor).astype(out[name].dtype)
    return out
```

```python
from contextlib import ExitStack

import concourse.bass as bass
from concourse import mybir

ALU = mybir.AluOpType
AX_X = mybir.AxisListType.X
F32 = mybir.dt.float32
I32 = mybir.dt.int32

P = 128
GROUP = 8
QUAD = 4
PAIR = 2
QUADS_PER_BLOCK = 8
GROUPS_PER_BLOCK = 4
X_SLOTS = 4
X_AHEAD = 3
XT_SLOTS = 2
BANKS = 4
CATS_PER_LOAD = 1
LOADS_IN_FLIGHT = 4
WEIGHT_SLOTS = 8
OUT_SLOTS = 4


def build_cond_residual(nc, x, cat, weights, bias, out):
    B, S, D = x.shape
    C, _, H = weights.shape
    K = D // P
    HALF = P // PAIR
    SPREAD = P // GROUP
    ROWS = S // SPREAD
    QUADS = B // QUAD
    BLOCKS = QUADS // QUADS_PER_BLOCK
    GROUPS = B // GROUP
    PAIRS = B // PAIR
    LOADS = C // CATS_PER_LOAD
    assert GROUPS_PER_BLOCK == X_SLOTS and B == P and S == HALF and D == H == 2 * P and SPREAD * ROWS == S

    x_rows = x.rearrange("b (a r) d -> (b a) (r d)", r=ROWS)
    out_rows = out.rearrange("b s h -> (b s) h")
    weight_loads = weights.rearrange("(n c) (k p) h -> n p c k h", c=CATS_PER_LOAD, p=P)

    with ExitStack() as ctx:
        def sb(name, shape, dt=F32):
            return ctx.enter_context(nc.sbuf_tensor(name, shape, dt))

        def sem(name):
            return ctx.enter_context(nc.semaphore(name))

        w_all = sb("w_all", [P, C, K, H])
        w_slot = sb("w_slot", [P, WEIGHT_SLOTS, K, H])
        x_nat = sb("x_nat", [P, X_SLOTS, ROWS, D])
        xT = sb("xT", [P, XT_SLOTS, K, GROUP, S])
        xbT = sb("xbT", [P, XT_SLOTS, K, GROUP, S])
        out_sb = sb("out_sb", [P, OUT_SLOTS, PAIR, H])

        ident = sb("ident", [P, P])
        zeros = sb("zeros", [P, P])
        iota_free = sb("iota_free", [P, P])
        iota_part = sb("iota_part", [P, 1])
        iota_part_i = sb("iota_part_i", [P, 1], I32)
        spread_i = sb("spread_i", [P, 1], I32)
        half_i = sb("half_i", [P, 1], I32)
        row_in_spread = sb("row_in_spread", [P, 1])
        row_in_half = sb("row_in_half", [P, 1])
        x_row0 = sb("x_row0", [P, 1])
        out_row0 = sb("out_row0", [P, 1])
        cat_row_i = sb("cat_row_i", [P, B], I32)
        cat_col_i = sb("cat_col_i", [P, 1], I32)
        cat_row = sb("cat_row", [P, B])
        cat_col = sb("cat_col", [P, 1])
        key_row = sb("key_row", [P, B])
        key_col = sb("key_col", [P, 1])
        smaller = sb("smaller", [P, B])
        rank = sb("rank", [P, 1])
        at_position = sb("at_position", [P, B])
        in_category = sb("in_category", [P, C])
        place_in_group = sb("place_in_group", [P, GROUP])
        which_group = sb("which_group", [P, GROUPS])
        place_in_pair = sb("place_in_pair", [P, PAIR])
        which_pair = sb("which_pair", [P, PAIRS])
        x_row_of = sb("x_row_of", [P, GROUP, SPREAD])
        out_row_of = sb("out_row_of", [P, PAIR, HALF])
        x_index = sb("x_index", [P, GROUPS], I32)
        out_index = sb("out_index", [P, PAIRS], I32)
        cat_sorted = sb("cat_sorted", [1, B], I32)
        sorted_in_category = sb("sorted_in_category", [C, B])
        bias_nat = sb("bias_nat", [C, H])
        bias_sorted = sb("bias_sorted", [P, K, B])

        xt_ps = [[ctx.enter_context(nc.psum_tensor(f"xt_ps{g}{k}", [P, ROWS, GROUP, SPREAD], F32))
                  for k in range(K)] for g in range(XT_SLOTS)]
        mm_ps = [ctx.enter_context(nc.psum_tensor(f"mm_ps{r}", [P, PAIR, H], F32))
                 for r in range(BANKS)]
        x_index_ps = mm_ps[0][:, 0, 0:GROUPS]
        out_index_ps = mm_ps[0][:, 1, 0:PAIRS]
        cat_sorted_ps = mm_ps[1][0:1, 0, 0:B]
        sorted_ps = mm_ps[2][0:C, 0, 0:B]
        bias_ps = mm_ps[3][:, 0, :].rearrange("p (k b) -> p k b", k=K)

        cats_loaded = sem("cats_loaded")
        bias_loaded = sem("bias_loaded")
        const_step = sem("const_step")
        consts_ready = sem("consts_ready")
        plan_step = sem("plan_step")
        plan_products = sem("plan_products")
        plan_read = sem("plan_read")
        w_loaded = [sem(f"w_loaded{n}") for n in range(LOADS_IN_FLIGHT)]
        w_loads_done = sem("w_loads_done")
        x_loaded = [sem(f"x_loaded{n}") for n in range(X_SLOTS)]
        halves_transposed = sem("halves_transposed")
        xT_ready = sem("xT_ready")
        xbT_ready = sem("xbT_ready")
        even_weights_ready = sem("even_weights_ready")
        odd_weights_ready = sem("odd_weights_ready")
        pairs_done = sem("pairs_done")
        quads_copied = sem("quads_copied")
        stored = [sem(f"stored{n}") for n in range(OUT_SLOTS)]

        block = ctx.enter_context(nc.Block())

        @block.sync
        def _(sp):
            sp.dma_start(cat_row_i[:, :], cat.partition_broadcast(P)).then_inc(cats_loaded, 16)
            sp.dma_start(cat_col_i[:, :], cat.rearrange("(b a) -> b a", a=1)).then_inc(cats_loaded, 16)

            def load(n, slot):
                at = bass.ds(n * CATS_PER_LOAD, CATS_PER_LOAD)
                sp.dma_start(w_all[:, at, :, :].rearrange("p c k h -> p (c k) h"),
                             weight_loads[bass.ds(n, 1)].rearrange("n p c k h -> p (n c k) h")
                             ).then_inc(w_loaded[slot], 16)

            def loaded(turn, slot):
                sp.wait_ge(w_loaded[slot], 16 * (turn + 1))
                sp.sem_inc(w_loads_done, 1)

            for slot in range(LOADS_IN_FLIGHT):
                load(slot, slot)
                if slot == 0:
                    sp.dma_start(bias_nat[:, :], bias).then_inc(bias_loaded, 16)
            with sp.Fori(1, LOADS // LOADS_IN_FLIGHT) as turn:
                for slot in range(LOADS_IN_FLIGHT):
                    loaded(turn - 1, slot)
                    load(turn * LOADS_IN_FLIGHT + slot, slot)
            for slot in range(LOADS_IN_FLIGHT):
                loaded(LOADS // LOADS_IN_FLIGHT - 1, slot)

        @block.gpsimd
        def _(pool):
            pool.iota(iota_free[:, :], [[1, P]], base=0, channel_multiplier=0,
                      allow_small_or_imprecise_dtypes=True).then_inc(consts_ready, 1)
            pool.iota(iota_part[:, :], [[0, 1]], base=0, channel_multiplier=1,
                      allow_small_or_imprecise_dtypes=True).then_inc(consts_ready, 1)
            pool.iota(iota_part_i[:, :], [[0, 1]], base=0, channel_multiplier=1).then_inc(consts_ready, 1)
            pool.memset(zeros[:, :], 0.0).then_inc(const_step, 1)
            pool.wait_ge(const_step, 1)
            pool.affine_select(out=ident[:, :], in_=zeros[:, :], compare_op=ALU.not_equal, fill=1.0, base=0,
                               pattern=[[-1, P]], channel_multiplier=1).then_inc(consts_ready, 1)

            def gather(g):
                if g >= X_SLOTS:
                    pool.wait_ge(halves_transposed, K * (g - X_SLOTS + 1))
                pool.indirect_dma_start(
                    x_nat[:, g % X_SLOTS, :, :].rearrange("p r d -> p (r d)"), None, x_rows,
                    bass.IndirectOffsetOnAxis(ap=x_index[:, g:g + 1], axis=0)
                ).then_inc(x_loaded[g % X_SLOTS], 16)

            def scatter(q):
                pool.wait_ge(quads_copied, q + 1)
                for p in range(PAIR):
                    t = PAIR * q + p
                    pool.indirect_dma_start(
                        out_rows, bass.IndirectOffsetOnAxis(ap=out_index[:, t:t + 1], axis=0),
                        out_sb[:, q % OUT_SLOTS, p, :], None).then_inc(stored[q % OUT_SLOTS], 16)

            pool.wait_ge(plan_read, 1)
            for g in range(X_AHEAD):
                gather(g)
            pool.wait_ge(plan_read, 2)
            for q in range(QUADS):
                g = q * QUAD // GROUP + X_AHEAD
                if q * QUAD % GROUP == 0 and g < GROUPS:
                    gather(g)
                if q >= 1:
                    scatter(q - 1)
            scatter(QUADS - 1)
            for s in stored:
                pool.wait_ge(s, 16 * PAIR * (QUADS // OUT_SLOTS))

        def copy_weights(eng, copy, t, r, p, half, ready):
            j = PAIR * t + half
            slot = (QUAD * ((r + 1) % QUADS_PER_BLOCK) + PAIR * p + half) % WEIGHT_SLOTS
            c = eng.value_load(cat_sorted[0:1, bass.ds(j, 1)], min_val=0, max_val=C - 1)
            eng.wait_ge(w_loads_done, c // CATS_PER_LOAD + 1)
            copy(w_slot[:, slot, :, :].rearrange("p k h -> p (k h)"),
                 w_all[:, bass.ds(c, 1), :, :].rearrange("p c k h -> p (c k h)")).then_inc(ready, 1)

        @block.scalar
        def _(act):
            def x_half(g, slot, k):
                act.wait_ge(halves_transposed, K * g + k + 1)
                nc.scalar.copy(xT[:, slot, k].rearrange("p j (a r) -> p r j a", r=ROWS),
                               xt_ps[slot][k][:, :, :, :]).then_inc(xT_ready, 1)

            def quad(it, r):
                q, g, k = QUADS_PER_BLOCK * it + r, GROUPS_PER_BLOCK * it + r // K, r % K
                static = isinstance(it, int)
                if not static or g + 1 < GROUPS:
                    if not static or g >= 1:
                        act.wait_ge(pairs_done, GROUP // PAIR * g)
                    x_half(g + 1, (r // K + 1) % XT_SLOTS, k)
                if not static or q + 1 < QUADS:
                    weights_of_next(it, r, q)

            def weights_of_next(it, r, q):
                for p in range(PAIR):
                    t = PAIR * (q + 1) + p
                    if not isinstance(it, int) or t >= WEIGHT_SLOTS // PAIR:
                        act.wait_ge(pairs_done, t - WEIGHT_SLOTS // PAIR + 1)
                    copy_weights(act, nc.scalar.copy, t, r, p, 1, odd_weights_ready)

            for k in range(K):
                x_half(0, 0, k)
            act.wait_ge(plan_read, 3)
            weights_of_next(0, QUADS_PER_BLOCK - 1, -1)
            for r in range(QUADS_PER_BLOCK):
                quad(0, r)
            with act.Fori(1, BLOCKS - 1) as it:
                for r in range(QUADS_PER_BLOCK):
                    quad(it, r)
            for r in range(QUADS_PER_BLOCK):
                quad(BLOCKS - 1, r)

        @block.vector
        def _(dve):
            steps = [0]

            def step(instruction):
                steps[0] += 1
                instruction.then_inc(plan_step, 1)
                dve.wait_ge(plan_step, steps[0])

            V = nc.vector
            dve.wait_ge(consts_ready, 3)
            V.tensor_single_scalar(spread_i[:, :], iota_part_i[:, :], SPREAD - 1, ALU.bitwise_and
                                   ).then_inc(plan_step, 1)
            V.tensor_single_scalar(half_i[:, :], iota_part_i[:, :], HALF - 1, ALU.bitwise_and
                                   ).then_inc(plan_step, 1)
            V.tensor_scalar(x_row0[:, :], iota_part[:, :], float(SPREAD), None, ALU.mult).then_inc(plan_step, 1)
            V.tensor_scalar(out_row0[:, :], iota_part[:, :], float(S), None, ALU.mult).then_inc(plan_step, 1)
            steps[0] += 4
            dve.wait_ge(plan_step, steps[0])
            V.tensor_copy(row_in_spread[:, :], spread_i[:, :]).then_inc(plan_step, 1)
            V.tensor_copy(row_in_half[:, :], half_i[:, :]).then_inc(plan_step, 1)
            steps[0] += 2
            dve.wait_ge(cats_loaded, 32)
            V.tensor_copy(cat_row[:, :], cat_row_i[:, :]).then_inc(plan_step, 1)
            steps[0] += 1
            step(V.tensor_copy(cat_col[:, :], cat_col_i[:, :]))
            V.scalar_tensor_tensor(out=key_row[:, :], in0=cat_row[:, :], scalar=float(B), in1=iota_free[:, :],
                                   op0=ALU.mult, op1=ALU.add).then_inc(plan_step, 1)
            steps[0] += 1
            step(V.scalar_tensor_tensor(out=key_col[:, :], in0=cat_col[:, :], scalar=float(B),
                                        in1=iota_part[:, :], op0=ALU.mult, op1=ALU.add))
            step(V.tensor_scalar(smaller[:, :], key_row[:, :], key_col[:, 0:1], None, ALU.is_lt))
            step(V.tensor_reduce(rank[:, :], smaller[:, :], AX_X, ALU.add))
            step(V.tensor_scalar(at_position[:, :], iota_free[:, :], rank[:, 0:1], None, ALU.is_equal))
            V.tensor_reduce(place_in_group[:, :], at_position[:, :].rearrange("p (g j) -> p j g", j=GROUP),
                            AX_X, ALU.add).then_inc(plan_step, 1)
            steps[0] += 1
            step(V.tensor_reduce(which_group[:, :], at_position[:, :].rearrange("p (g j) -> p g j", j=GROUP),
                                 AX_X, ALU.add))
            step(V.tensor_scalar(x_row_of[:, :, :],
                                 place_in_group[:, :].unsqueeze(2).broadcast_to([P, GROUP, SPREAD]),
                                 x_row0[:, 0:1], None, ALU.mult))
            X_PLAN = steps[0]
            V.tensor_scalar(in_category[:, :], iota_free[:, 0:C], cat_col[:, 0:1], None, ALU.is_equal
                            ).then_inc(plan_step, 1)
            V.tensor_reduce(place_in_pair[:, :], at_position[:, :].rearrange("p (t j) -> p j t", j=PAIR),
                            AX_X, ALU.add).then_inc(plan_step, 1)
            steps[0] += 2
            step(V.tensor_reduce(which_pair[:, :], at_position[:, :].rearrange("p (t j) -> p t j", j=PAIR),
                                 AX_X, ALU.add))
            assert (X_PLAN, steps[0]) == (plan["x"], plan["categories"])
            dve.wait_ge(plan_products, 1)
            V.tensor_scalar(x_index[:, :], x_index_ps, row_in_spread[:, 0:1], None, ALU.add
                            ).then_inc(plan_read, 1)
            step(V.tensor_scalar(out_row_of[:, :, :],
                                 place_in_pair[:, :].unsqueeze(2).broadcast_to([P, PAIR, HALF]),
                                 out_row0[:, 0:1], None, ALU.mult))
            assert steps[0] == plan["out"]
            dve.wait_ge(plan_products, 3)
            step(V.tensor_copy(sorted_in_category[:, :], sorted_ps))
            assert steps[0] == plan["sorted"]
            dve.wait_ge(plan_products, 4)
            V.tensor_scalar(out_index[:, :], out_index_ps, row_in_half[:, 0:1], None, ALU.add
                            ).then_inc(plan_read, 1)
            V.tensor_copy(cat_sorted[:, :], cat_sorted_ps).then_inc(plan_read, 1)
            dve.wait_ge(plan_products, 5)
            V.tensor_copy(bias_sorted[:, :, :], bias_ps).then_inc(plan_read, 1)

            def xb_half(g, slot, k):
                dve.wait_ge(xT_ready, K * g + k + 1)
                V.tensor_tensor(
                    xbT[:, slot, k].rearrange("p j (a r) -> p r j a", r=ROWS), xt_ps[slot][k][:, :, :, :],
                    bias_sorted[:, k, bass.ds(GROUP * g, GROUP)].unsqueeze(1).unsqueeze(3).broadcast_to(
                        [P, ROWS, GROUP, SPREAD]), ALU.add).then_inc(xbT_ready, 1)

            def copy_out(slot, q):
                dve.wait_ge(pairs_done, PAIR * (q + 1))
                V.tensor_copy(out_sb[:, slot, :, :], mm_ps[slot][:, :, :]).then_inc(quads_copied, 1)

            def quad(it, r):
                q, g, k = QUADS_PER_BLOCK * it + r, GROUPS_PER_BLOCK * it + r // K, r % K
                static = isinstance(it, int)
                if not static or g + 1 < GROUPS:
                    if not static or g >= 1:
                        dve.wait_ge(pairs_done, GROUP // PAIR * g)
                    xb_half(g + 1, (r // K + 1) % XT_SLOTS, k)
                if not static or q + 1 < QUADS:
                    weights_of_next(it, r, q)
                if not static or q >= 1:
                    turn = QUADS_PER_BLOCK // OUT_SLOTS * it + (r - 1) // OUT_SLOTS
                    if not static or turn >= 1:
                        dve.wait_ge(stored[(r - 1) % OUT_SLOTS], 16 * PAIR * turn)
                    copy_out((r - 1) % OUT_SLOTS, q - 1)

            def weights_of_next(it, r, q):
                for p in range(PAIR):
                    t = PAIR * (q + 1) + p
                    if not isinstance(it, int) or t >= WEIGHT_SLOTS // PAIR:
                        dve.wait_ge(pairs_done, t - WEIGHT_SLOTS // PAIR + 1)
                    copy_weights(dve, V.tensor_copy, t, r, p, 0, even_weights_ready)

            dve.wait_ge(plan_read, 4)
            for k in range(K):
                xb_half(0, 0, k)
            weights_of_next(0, QUADS_PER_BLOCK - 1, -1)
            for r in range(QUADS_PER_BLOCK):
                quad(0, r)
            with dve.Fori(1, BLOCKS - 1) as it:
                for r in range(QUADS_PER_BLOCK):
                    quad(it, r)
            for r in range(QUADS_PER_BLOCK):
                quad(BLOCKS - 1, r)
            dve.wait_ge(stored[OUT_SLOTS - 1], 16 * PAIR * (QUADS // OUT_SLOTS - 1))
            copy_out(OUT_SLOTS - 1, QUADS - 1)

        @block.tensor
        def _(pe):
            T = nc.tensor

            pe.wait_ge(plan_step, plan["x"])
            T.matmul(x_index_ps, x_row_of[:, :, :].rearrange("p j a -> p (j a)"), which_group[:, :],
                     start=True, stop=True).then_inc(plan_products, 1)
            pe.wait_ge(plan_step, plan["categories"])
            T.matmul(cat_sorted_ps, cat_col[:, :], at_position[:, :], start=True, stop=True
                     ).then_inc(plan_products, 1)
            T.matmul(sorted_ps, in_category[:, :], at_position[:, :], start=True, stop=True
                     ).then_inc(plan_products, 1)
            pe.wait_ge(plan_step, plan["out"])
            pe.wait_ge(plan_read, 1)
            T.matmul(out_index_ps, out_row_of[:, :, :].rearrange("p j a -> p (j a)"), which_pair[:, :],
                     start=True, stop=True).then_inc(plan_products, 1)
            pe.wait_ge(plan_step, plan["sorted"])
            pe.wait_ge(bias_loaded, 16)
            for k in range(K):
                last = T.matmul(bias_ps[:, k, :], bias_nat[:, k * P:(k + 1) * P], sorted_in_category[:, :],
                                start=True, stop=True)
            last.then_inc(plan_products, 1)

            def transpose_half(x_slot, slot, k):
                for r in range(ROWS):
                    last = T.transpose(xt_ps[slot][k][:, r, :, :].rearrange("p j a -> p (j a)"),
                                       x_nat[:, x_slot, r, k * P:(k + 1) * P], ident[:, :])
                last.then_inc(halves_transposed, 1)

            def quad(it, r):
                q, g, k = QUADS_PER_BLOCK * it + r, GROUPS_PER_BLOCK * it + r // K, r % K
                static = isinstance(it, int)
                slot, next_slot = (r // K) % XT_SLOTS, (r // K + 1) % XT_SLOTS
                bank = r % BANKS
                if not static or g + 1 < GROUPS:
                    if k == 0:
                        x_slot = (r // K + 1) % X_SLOTS
                        turn = it + (r // K + 1) // X_SLOTS
                        pe.wait_ge(x_loaded[x_slot], 16 * (turn + 1))
                    if not static or q >= 2:
                        pe.wait_ge(xbT_ready, q - 1)
                    transpose_half((r // K + 1) % X_SLOTS, next_slot, k)
                if not static or q >= BANKS:
                    pe.wait_ge(quads_copied, q - BANKS + 1)
                if k == 0:
                    pe.wait_ge(xbT_ready, K * g + K)
                for p in range(PAIR):
                    j = (QUAD * r + PAIR * p) % GROUP
                    for kk in range(K):
                        T.matmul(mm_ps[bank][:, p, kk * P:(kk + 1) * P],
                                 xbT[:, slot, kk, j:j + PAIR, :].rearrange("p j s -> p (j s)"), ident[:, :],
                                 start=(p == 0 and kk == 0), stop=False, is_transpose=True, skip_group_check=True)
                for p in range(PAIR):
                    t = PAIR * q + p
                    pe.wait_ge(even_weights_ready, t + 1)
                    pe.wait_ge(odd_weights_ready, t + 1)
                    for kk in range(K):
                        for half in range(PAIR):
                            j = QUAD * r + PAIR * p + half
                            last = T.matmul(mm_ps[bank][HALF * half:HALF * (half + 1), p, :],
                                            xT[:, slot, kk, j % GROUP, :], w_slot[:, j % WEIGHT_SLOTS, kk, :],
                                            start=False, stop=(kk == K - 1), skip_group_check=True)
                    last.then_inc(pairs_done, 1)

            pe.wait_ge(consts_ready, 4)
            pe.wait_ge(x_loaded[0], 16)
            for k in range(K):
                transpose_half(0, 0, k)
            pe.wait_ge(plan_read, 4)
            for r in range(QUADS_PER_BLOCK):
                quad(0, r)
            with pe.Fori(1, BLOCKS - 1) as it:
                for r in range(QUADS_PER_BLOCK):
                    quad(it, r)
            for r in range(QUADS_PER_BLOCK):
                quad(BLOCKS - 1, r)


plan = {"x": 16, "categories": 19, "out": 20, "sorted": 21}

_INS = ["x", "itok_B_0_63", "L0_cond_W", "L0_cond_b"]


def kernel(**inputs):
    import numpy as np
    import concourse.bacc as bacc
    from concourse.bass_utils import run_bass_kernel_spmd

    nc = bacc.Bacc("TRN2", target_bir_lowering=False, num_devices=1)
    arrays, args = {}, []
    for name in _INS:
        a = np.ascontiguousarray(inputs[name])
        arrays[f"in_{name}"] = a
        args.append(nc.dram_tensor(f"in_{name}", a.shape, mybir.dt.from_np(a.dtype), kind="ExternalInput").ap())
    shape = inputs["x"].shape
    out = nc.dram_tensor("out", shape, mybir.dt.float32, kind="ExternalOutput").ap()
    build_cond_residual(nc, *args, out)
    result = run_bass_kernel_spmd(nc, [arrays], core_ids=[0])
    return result.results[0]["out"]
```

```python
from contextlib import ExitStack

import concourse.bass as bass
from concourse import mybir

ALU = mybir.AluOpType
AX_X = mybir.AxisListType.X
F32 = mybir.dt.float32
I32 = mybir.dt.int32

P = 128
GROUP = 8
QUAD = 4
PAIR = 2
QUADS_PER_BLOCK = 8
GROUPS_PER_BLOCK = 4
X_SLOTS = 4
X_AHEAD = 3
XT_SLOTS = 2
BANKS = 4
CATS_PER_LOAD = 1
LOADS_IN_FLIGHT = 4
WEIGHT_SLOTS = 8
OUT_SLOTS = 4
WARM_UP = 9


def build_cond_residual(nc, x, cat, weights, bias, out):
    B, S, D = x.shape
    C, _, H = weights.shape
    K = D // P
    HALF = P // PAIR
    SPREAD = P // GROUP
    ROWS = S // SPREAD
    QUADS = B // QUAD
    BLOCKS = QUADS // QUADS_PER_BLOCK
    GROUPS = B // GROUP
    PAIRS = B // PAIR
    LOADS = C // CATS_PER_LOAD
    assert GROUPS_PER_BLOCK == X_SLOTS and B == P and S == HALF and D == H == 2 * P and SPREAD * ROWS == S

    x_rows = x.rearrange("b (a r) d -> (b a) (r d)", r=ROWS)
    out_rows = out.rearrange("b s h -> (b s) h")
    weight_loads = weights.rearrange("(n c) (k p) h -> n p c k h", c=CATS_PER_LOAD, p=P)

    with ExitStack() as ctx:
        def sb(name, shape, dt=F32):
            return ctx.enter_context(nc.sbuf_tensor(name, shape, dt))

        def sem(name):
            return ctx.enter_context(nc.semaphore(name))

        w_all = sb("w_all", [P, C, K, H])
        w_slot = sb("w_slot", [P, WEIGHT_SLOTS, K, H])
        x_nat = sb("x_nat", [P, X_SLOTS, ROWS, D])
        xT = sb("xT", [P, XT_SLOTS, K, GROUP, S])
        xbT = sb("xbT", [P, XT_SLOTS, K, GROUP, S])
        out_sb = sb("out_sb", [P, OUT_SLOTS, PAIR, H])

        ident = sb("ident", [P, P])
        zeros = sb("zeros", [P, P])
        iota_free = sb("iota_free", [P, P])
        iota_part = sb("iota_part", [P, 1])
        iota_part_i = sb("iota_part_i", [P, 1], I32)
        spread_i = sb("spread_i", [P, 1], I32)
        half_i = sb("half_i", [P, 1], I32)
        row_in_spread = sb("row_in_spread", [P, 1])
        row_in_half = sb("row_in_half", [P, 1])
        x_row0 = sb("x_row0", [P, 1])
        out_row0 = sb("out_row0", [P, 1])
        cat_row_i = sb("cat_row_i", [P, B], I32)
        cat_col_i = sb("cat_col_i", [P, 1], I32)
        cat_col = sb("cat_col", [P, 1])
        key_row = sb("key_row", [P, B])
        key_col = sb("key_col", [P, 1])
        smaller = sb("smaller", [P, B])
        rank = sb("rank", [P, 1])
        at_position = sb("at_position", [P, B])
        in_category = sb("in_category", [P, C])
        place_in_group = sb("place_in_group", [P, GROUP])
        which_group = sb("which_group", [P, GROUPS])
        place_in_pair = sb("place_in_pair", [P, PAIR])
        which_pair = sb("which_pair", [P, PAIRS])
        x_row_of = sb("x_row_of", [P, GROUP, SPREAD])
        out_row_of = sb("out_row_of", [P, PAIR, HALF])
        x_index = sb("x_index", [P, GROUPS], I32)
        out_index = sb("out_index", [P, PAIRS], I32)
        cat_sorted = sb("cat_sorted", [1, B], I32)
        sorted_in_category = sb("sorted_in_category", [C, B])
        bias_nat = sb("bias_nat", [C, H])
        bias_sorted = sb("bias_sorted", [P, K, B])

        xt_ps = [[ctx.enter_context(nc.psum_tensor(f"xt_ps{g}{k}", [P, ROWS, GROUP, SPREAD], F32))
                  for k in range(K)] for g in range(XT_SLOTS)]
        mm_ps = [ctx.enter_context(nc.psum_tensor(f"mm_ps{r}", [P, PAIR, H], F32))
                 for r in range(BANKS)]
        last_pair_ps = xt_ps[GROUPS % XT_SLOTS][0][:, :, :, :].rearrange("p r j a -> p (r j a)")[:, 0:H]
        x_index_ps = mm_ps[0][:, 0, 0:GROUPS]
        out_index_ps = mm_ps[0][:, 1, 0:PAIRS]
        cat_sorted_ps = mm_ps[1][0:1, 0, 0:B]
        sorted_ps = mm_ps[2][0:C, 0, 0:B]
        bias_ps = mm_ps[3][:, 0, :].rearrange("p (k b) -> p k b", k=K)

        cats_loaded = sem("cats_loaded")
        bias_loaded = sem("bias_loaded")
        const_step = sem("const_step")
        consts_ready = sem("consts_ready")
        plan_step = sem("plan_step")
        plan_products = sem("plan_products")
        plan_read = sem("plan_read")
        w_loaded = [sem(f"w_loaded{n}") for n in range(LOADS_IN_FLIGHT)]
        w_loads_done = sem("w_loads_done")
        x_loaded = [sem(f"x_loaded{n}") for n in range(X_SLOTS)]
        halves_transposed = sem("halves_transposed")
        xT_ready = sem("xT_ready")
        xbT_ready = sem("xbT_ready")
        even_weights_ready = sem("even_weights_ready")
        odd_weights_ready = sem("odd_weights_ready")
        pairs_done = sem("pairs_done")
        quads_copied = sem("quads_copied")
        stored = [sem(f"stored{n}") for n in range(OUT_SLOTS)]

        block = ctx.enter_context(nc.Block())

        @block.sync
        def _(sp):
            sp.dma_start(cat_row_i[:, :], cat.partition_broadcast(P)).then_inc(cats_loaded, 16)
            sp.dma_start(cat_col_i[:, :], cat.rearrange("(b a) -> b a", a=1)).then_inc(cats_loaded, 16)

            def load(n, slot):
                at = bass.ds(n * CATS_PER_LOAD, CATS_PER_LOAD)
                sp.dma_start(w_all[:, at, :, :].rearrange("p c k h -> p (c k) h"),
                             weight_loads[bass.ds(n, 1)].rearrange("n p c k h -> p (n c k) h")
                             ).then_inc(w_loaded[slot], 16)

            def loaded(turn, slot):
                sp.wait_ge(w_loaded[slot], 16 * (turn + 1))
                sp.sem_inc(w_loads_done, 1)

            for slot in range(LOADS_IN_FLIGHT):
                load(slot, slot)
                if slot == 0:
                    sp.dma_start(bias_nat[:, :], bias).then_inc(bias_loaded, 16)
            with sp.Fori(1, LOADS // LOADS_IN_FLIGHT) as turn:
                for slot in range(LOADS_IN_FLIGHT):
                    loaded(turn - 1, slot)
                    load(turn * LOADS_IN_FLIGHT + slot, slot)
            for slot in range(LOADS_IN_FLIGHT):
                loaded(LOADS // LOADS_IN_FLIGHT - 1, slot)

        @block.gpsimd
        def _(pool):
            pool.iota(iota_free[:, :], [[1, P]], base=0, channel_multiplier=0,
                      allow_small_or_imprecise_dtypes=True).then_inc(consts_ready, 1)
            pool.iota(iota_part[:, :], [[0, 1]], base=0, channel_multiplier=1,
                      allow_small_or_imprecise_dtypes=True).then_inc(consts_ready, 1)
            pool.iota(iota_part_i[:, :], [[0, 1]], base=0, channel_multiplier=1).then_inc(consts_ready, 1)
            pool.memset(zeros[:, :], 0.0).then_inc(const_step, 1)
            pool.wait_ge(const_step, 1)
            pool.affine_select(out=ident[:, :], in_=zeros[:, :], compare_op=ALU.not_equal, fill=1.0, base=0,
                               pattern=[[-1, P]], channel_multiplier=1).then_inc(consts_ready, 1)

            def gather(g):
                if g >= X_SLOTS:
                    pool.wait_ge(halves_transposed, K * (g - X_SLOTS + 1))
                pool.indirect_dma_start(
                    x_nat[:, g % X_SLOTS, :, :].rearrange("p r d -> p (r d)"), None, x_rows,
                    bass.IndirectOffsetOnAxis(ap=x_index[:, g:g + 1], axis=0)
                ).then_inc(x_loaded[g % X_SLOTS], 16)

            def scatter(q):
                if q < QUADS - 1:
                    pool.wait_ge(quads_copied, q + 1)
                for p in range(PAIR):
                    t = PAIR * q + p
                    if q == QUADS - 1:
                        pool.wait_ge(quads_copied, q + p + 1)
                    pool.indirect_dma_start(
                        out_rows, bass.IndirectOffsetOnAxis(ap=out_index[:, t:t + 1], axis=0),
                        out_sb[:, q % OUT_SLOTS, p, :], None).then_inc(stored[q % OUT_SLOTS], 16)

            pool.wait_ge(plan_read, 1)
            for g in range(X_AHEAD):
                gather(g)
            pool.wait_ge(plan_read, 2)
            for q in range(QUADS):
                g = q * QUAD // GROUP + X_AHEAD
                if q * QUAD % GROUP == 0 and g < GROUPS:
                    gather(g)
                if q >= 1:
                    scatter(q - 1)
            scatter(QUADS - 1)
            for s in stored:
                pool.wait_ge(s, 16 * PAIR * (QUADS // OUT_SLOTS))

        def copy_weights(eng, copy, t, r, p, half, ready):
            j = PAIR * t + half
            slot = (QUAD * ((r + 1) % QUADS_PER_BLOCK) + PAIR * p + half) % WEIGHT_SLOTS
            c = eng.value_load(cat_sorted[0:1, bass.ds(j, 1)], min_val=0, max_val=C - 1)
            eng.wait_ge(w_loads_done, c // CATS_PER_LOAD + 1)
            copy(w_slot[:, slot, :, :].rearrange("p k h -> p (k h)"),
                 w_all[:, bass.ds(c, 1), :, :].rearrange("p c k h -> p (c k h)")).then_inc(ready, 1)

        @block.scalar
        def _(act):
            def x_half(g, slot, k):
                act.wait_ge(halves_transposed, K * g + k + 1)
                nc.scalar.copy(xT[:, slot, k].rearrange("p j (a r) -> p r j a", r=ROWS),
                               xt_ps[slot][k][:, :, :, :]).then_inc(xT_ready, 1)

            def quad(it, r):
                q, g, k = QUADS_PER_BLOCK * it + r, GROUPS_PER_BLOCK * it + r // K, r % K
                static = isinstance(it, int)
                if not static or g + 1 < GROUPS:
                    if not static or g >= 1:
                        act.wait_ge(pairs_done, GROUP // PAIR * g)
                    x_half(g + 1, (r // K + 1) % XT_SLOTS, k)
                if not static or q + 1 < QUADS:
                    weights_of_next(it, r, q)

            def weights_of_next(it, r, q):
                for p in range(PAIR):
                    t = PAIR * (q + 1) + p
                    if not isinstance(it, int) or t >= WEIGHT_SLOTS // PAIR:
                        act.wait_ge(pairs_done, t - WEIGHT_SLOTS // PAIR + 1)
                    copy_weights(act, nc.scalar.copy, t, r, p, 1, odd_weights_ready)

            for k in range(K):
                x_half(0, 0, k)
            act.wait_ge(plan_read, 3)
            weights_of_next(0, QUADS_PER_BLOCK - 1, -1)
            for r in range(QUADS_PER_BLOCK):
                quad(0, r)
            with act.Fori(1, BLOCKS - 1) as it:
                for r in range(QUADS_PER_BLOCK):
                    quad(it, r)
            for r in range(QUADS_PER_BLOCK):
                quad(BLOCKS - 1, r)

        @block.vector
        def _(dve):
            steps = [0]

            def step(instruction):
                steps[0] += 1
                instruction.then_inc(plan_step, 1)
                dve.wait_ge(plan_step, steps[0])

            V = nc.vector
            dve.wait_ge(consts_ready, 3)
            V.tensor_single_scalar(spread_i[:, :], iota_part_i[:, :], SPREAD - 1, ALU.bitwise_and
                                   ).then_inc(plan_step, 1)
            V.tensor_single_scalar(half_i[:, :], iota_part_i[:, :], HALF - 1, ALU.bitwise_and
                                   ).then_inc(plan_step, 1)
            V.tensor_scalar(x_row0[:, :], iota_part[:, :], float(SPREAD), None, ALU.mult).then_inc(plan_step, 1)
            V.tensor_scalar(out_row0[:, :], iota_part[:, :], float(S), None, ALU.mult).then_inc(plan_step, 1)
            steps[0] += 4
            dve.wait_ge(plan_step, steps[0])
            V.tensor_copy(row_in_spread[:, :], spread_i[:, :]).then_inc(plan_step, 1)
            V.tensor_copy(row_in_half[:, :], half_i[:, :]).then_inc(plan_step, 1)
            steps[0] += 2
            dve.wait_ge(cats_loaded, 32)
            V.tensor_copy(cat_col[:, :], cat_col_i[:, :]).then_inc(plan_step, 1)
            steps[0] += 1
            V.scalar_tensor_tensor(out=key_row[:, :], in0=cat_row_i[:, :], scalar=float(B), in1=iota_free[:, :],
                                   op0=ALU.mult, op1=ALU.add).then_inc(plan_step, 1)
            steps[0] += 1
            step(V.scalar_tensor_tensor(out=key_col[:, :], in0=cat_col_i[:, :], scalar=float(B),
                                        in1=iota_part[:, :], op0=ALU.mult, op1=ALU.add))
            step(V.tensor_scalar(smaller[:, :], key_row[:, :], key_col[:, 0:1], 0.0, ALU.is_lt, ALU.add,
                                 accum_out=rank[:, 0:1]))
            step(V.tensor_scalar(at_position[:, :], iota_free[:, :], rank[:, 0:1], None, ALU.is_equal))
            V.tensor_reduce(place_in_group[:, :], at_position[:, :].rearrange("p (g j) -> p j g", j=GROUP),
                            AX_X, ALU.add).then_inc(plan_step, 1)
            steps[0] += 1
            step(V.tensor_reduce(which_group[:, :], at_position[:, :].rearrange("p (g j) -> p g j", j=GROUP),
                                 AX_X, ALU.add))
            step(V.tensor_scalar(x_row_of[:, :, :],
                                 place_in_group[:, :].unsqueeze(2).broadcast_to([P, GROUP, SPREAD]),
                                 x_row0[:, 0:1], None, ALU.mult))
            X_PLAN = steps[0]
            V.tensor_scalar(in_category[:, :], iota_free[:, 0:C], cat_col[:, 0:1], None, ALU.is_equal
                            ).then_inc(plan_step, 1)
            V.tensor_reduce(place_in_pair[:, :], at_position[:, :].rearrange("p (t j) -> p j t", j=PAIR),
                            AX_X, ALU.add).then_inc(plan_step, 1)
            steps[0] += 2
            step(V.tensor_reduce(which_pair[:, :], at_position[:, :].rearrange("p (t j) -> p t j", j=PAIR),
                                 AX_X, ALU.add))
            assert (X_PLAN, steps[0]) == (plan["x"], plan["categories"])
            dve.wait_ge(plan_products, 1)
            V.tensor_scalar(x_index[:, :], x_index_ps, row_in_spread[:, 0:1], None, ALU.add
                            ).then_inc(plan_read, 1)
            step(V.tensor_scalar(out_row_of[:, :, :],
                                 place_in_pair[:, :].unsqueeze(2).broadcast_to([P, PAIR, HALF]),
                                 out_row0[:, 0:1], None, ALU.mult))
            assert steps[0] == plan["out"]
            dve.wait_ge(plan_products, 3)
            step(V.tensor_copy(sorted_in_category[:, :], sorted_ps))
            assert steps[0] == plan["sorted"]
            dve.wait_ge(plan_products, 4)
            V.tensor_scalar(out_index[:, :], out_index_ps, row_in_half[:, 0:1], None, ALU.add
                            ).then_inc(plan_read, 1)
            V.tensor_copy(cat_sorted[:, :], cat_sorted_ps).then_inc(plan_read, 1)
            dve.wait_ge(plan_products, 5)
            V.tensor_copy(bias_sorted[:, :, :], bias_ps).then_inc(plan_read, 1)

            def xb_half(g, slot, k):
                dve.wait_ge(xT_ready, K * g + k + 1)
                V.tensor_tensor(
                    xbT[:, slot, k].rearrange("p j (a r) -> p r j a", r=ROWS), xt_ps[slot][k][:, :, :, :],
                    bias_sorted[:, k, bass.ds(GROUP * g, GROUP)].unsqueeze(1).unsqueeze(3).broadcast_to(
                        [P, ROWS, GROUP, SPREAD]), ALU.add).then_inc(xbT_ready, 1)

            def copy_out(slot, q):
                dve.wait_ge(pairs_done, PAIR * (q + 1))
                V.tensor_copy(out_sb[:, slot, :, :], mm_ps[slot][:, :, :]).then_inc(quads_copied, 1)

            def quad(it, r):
                q, g, k = QUADS_PER_BLOCK * it + r, GROUPS_PER_BLOCK * it + r // K, r % K
                static = isinstance(it, int)
                if not static or g + 1 < GROUPS:
                    if not static or g >= 1:
                        dve.wait_ge(pairs_done, GROUP // PAIR * g)
                    xb_half(g + 1, (r // K + 1) % XT_SLOTS, k)
                if not static or q + 1 < QUADS:
                    weights_of_next(it, r, q)
                if not static or q >= 1:
                    turn = QUADS_PER_BLOCK // OUT_SLOTS * it + (r - 1) // OUT_SLOTS
                    if not static or turn >= 1:
                        dve.wait_ge(stored[(r - 1) % OUT_SLOTS], 16 * PAIR * turn)
                    copy_out((r - 1) % OUT_SLOTS, q - 1)

            def weights_of_next(it, r, q):
                for p in range(PAIR):
                    t = PAIR * (q + 1) + p
                    if not isinstance(it, int) or t >= WEIGHT_SLOTS // PAIR:
                        dve.wait_ge(pairs_done, t - WEIGHT_SLOTS // PAIR + 1)
                    copy_weights(dve, V.tensor_copy, t, r, p, 0, even_weights_ready)

            dve.wait_ge(plan_read, 4)
            for k in range(K):
                xb_half(0, 0, k)
            weights_of_next(0, QUADS_PER_BLOCK - 1, -1)
            for r in range(QUADS_PER_BLOCK):
                quad(0, r)
            with dve.Fori(1, BLOCKS - 1) as it:
                for r in range(QUADS_PER_BLOCK):
                    quad(it, r)
            for r in range(QUADS_PER_BLOCK):
                quad(BLOCKS - 1, r)
            dve.wait_ge(stored[OUT_SLOTS - 1], 16 * PAIR * (QUADS // OUT_SLOTS - 1))
            for p in range(PAIR):
                dve.wait_ge(pairs_done, PAIRS - PAIR + p + 1)
                V.tensor_copy(out_sb[:, OUT_SLOTS - 1, p, :], (mm_ps[BANKS - 1][:, 0, :], last_pair_ps)[p]
                              ).then_inc(quads_copied, 1)

        @block.tensor
        def _(pe):
            T = nc.tensor

            pe.wait_ge(plan_step, plan["x"])
            T.matmul(x_index_ps, x_row_of[:, :, :].rearrange("p j a -> p (j a)"), which_group[:, :],
                     start=True, stop=True).then_inc(plan_products, 1)
            pe.wait_ge(plan_step, plan["categories"])
            T.matmul(cat_sorted_ps, cat_col[:, :], at_position[:, :], start=True, stop=True
                     ).then_inc(plan_products, 1)
            T.matmul(sorted_ps, in_category[:, :], at_position[:, :], start=True, stop=True
                     ).then_inc(plan_products, 1)
            pe.wait_ge(plan_step, plan["out"])
            pe.wait_ge(plan_read, 1)
            T.matmul(out_index_ps, out_row_of[:, :, :].rearrange("p j a -> p (j a)"), which_pair[:, :],
                     start=True, stop=True).then_inc(plan_products, 1)
            pe.wait_ge(plan_step, plan["sorted"])
            pe.wait_ge(bias_loaded, 16)
            for k in range(K):
                last = T.matmul(bias_ps[:, k, :], bias_nat[:, k * P:(k + 1) * P], sorted_in_category[:, :],
                                start=True, stop=True)
            last.then_inc(plan_products, 1)

            def transpose_half(x_slot, slot, k):
                for r in range(ROWS):
                    last = T.transpose(xt_ps[slot][k][:, r, :, :].rearrange("p j a -> p (j a)"),
                                       x_nat[:, x_slot, r, k * P:(k + 1) * P], ident[:, :])
                last.then_inc(halves_transposed, 1)

            def group(it, r):
                g = GROUPS_PER_BLOCK * it + r
                static = isinstance(it, int)

                def sums(quad, p):
                    if static and (g, quad, p) == (GROUPS - 1, GROUP // QUAD - 1, PAIR - 1):
                        return last_pair_ps
                    return mm_ps[(GROUP // QUAD * r + quad) % BANKS][:, p, :]

                x_slot, slot, next_slot = (r + 1) % X_SLOTS, r % XT_SLOTS, (r + 1) % XT_SLOTS
                if not static or g + 1 < GROUPS:
                    pe.wait_ge(x_loaded[x_slot], 16 * (it + (r + 1) // X_SLOTS + 1))
                    for k in range(K):
                        if not static or g + 1 >= XT_SLOTS:
                            pe.wait_ge(xbT_ready, K * (g + 1 - XT_SLOTS) + k + 1)
                        transpose_half(x_slot, next_slot, k)
                pe.wait_ge(xbT_ready, K * g + K)
                for quad in range(GROUP // QUAD):
                    q = GROUP // QUAD * g + quad
                    if not static or q >= BANKS:
                        pe.wait_ge(quads_copied, q - BANKS + 1)
                    for p in range(PAIR):
                        j = QUAD * quad + PAIR * p
                        to = sums(quad, p)
                        for k in range(K):
                            T.matmul(to[:, k * P:(k + 1) * P],
                                     xbT[:, slot, k, j:j + PAIR, :].rearrange("p j s -> p (j s)"), ident[:, :],
                                     start=(k == 0 and (p == 0 or to is last_pair_ps)), stop=False, is_transpose=True,
                                     skip_group_check=True)
                for pair in range(GROUP // PAIR):
                    t = GROUP // PAIR * g + pair
                    to = sums(pair // PAIR, pair % PAIR)
                    pe.wait_ge(even_weights_ready, t + 1)
                    pe.wait_ge(odd_weights_ready, t + 1)
                    for k in range(K):
                        for half in range(PAIR):
                            j = PAIR * pair + half
                            last = T.matmul(to[HALF * half:HALF * (half + 1), :],
                                            xT[:, slot, k, j, :], w_slot[:, (GROUP * r + j) % WEIGHT_SLOTS, k, :],
                                            start=False, stop=(k == K - 1), skip_group_check=True)
                    last.then_inc(pairs_done, 1)

            pe.wait_ge(consts_ready, 4)
            for _ in range(WARM_UP):
                T.transpose(xt_ps[1][0][:, 0, :, :].rearrange("p j a -> p (j a)"), ident[:, :], ident[:, :])
            pe.wait_ge(x_loaded[0], 16)
            for k in range(K):
                transpose_half(0, 0, k)
            pe.wait_ge(plan_read, 4)
            for r in range(GROUPS_PER_BLOCK):
                group(0, r)
            with pe.Fori(1, BLOCKS - 1) as it:
                for r in range(GROUPS_PER_BLOCK):
                    group(it, r)
            for r in range(GROUPS_PER_BLOCK):
                group(BLOCKS - 1, r)


plan = {"x": 14, "categories": 17, "out": 18, "sorted": 19}

_INS = ["x", "itok_B_0_63", "L0_cond_W", "L0_cond_b"]


def kernel(**inputs):
    import numpy as np
    import concourse.bacc as bacc
    from concourse.bass_utils import run_bass_kernel_spmd

    nc = bacc.Bacc("TRN2", target_bir_lowering=False, num_devices=1)
    arrays, args = {}, []
    for name in _INS:
        a = np.ascontiguousarray(inputs[name])
        arrays[f"in_{name}"] = a
        args.append(nc.dram_tensor(f"in_{name}", a.shape, mybir.dt.from_np(a.dtype), kind="ExternalInput").ap())
    shape = inputs["x"].shape
    out = nc.dram_tensor("out", shape, mybir.dt.float32, kind="ExternalOutput").ap()
    build_cond_residual(nc, *args, out)
    result = run_bass_kernel_spmd(nc, [arrays], core_ids=[0])
    return result.results[0]["out"]
```

```python
from contextlib import ExitStack

import concourse.bass as bass
from concourse import mybir

ALU = mybir.AluOpType
AX_X = mybir.AxisListType.X
F32 = mybir.dt.float32
I32 = mybir.dt.int32

P = 128
GROUP = 8
QUAD = 4
PAIR = 2
X_SLOTS = 4
X_AHEAD = 3
XT_SLOTS = 2
BANKS = 4
WEIGHT_SLOTS = 8
OUT_SLOTS = 4
GROUPS_PER_BLOCK = X_SLOTS
QUADS_PER_BLOCK = GROUPS_PER_BLOCK * GROUP // QUAD
LOADS_IN_FLIGHT = 4
UNCHECKED_LOADS = 6
WARM_UP = (3, 5)
SHARED_FROM, SHARED_TO = 4, 1

PLAN_STEPS = {"x": 15, "categories": 19, "out": 20, "sorted": 21}


def build_cond_residual(nc, x, cat, weights, bias, out):
    B, S, D = x.shape
    C, _, H = weights.shape
    K = D // P
    HALF = P // PAIR
    SPREAD = P // GROUP
    ROWS = S // SPREAD
    QUADS = B // QUAD
    BLOCKS = QUADS // QUADS_PER_BLOCK
    GROUPS = B // GROUP
    PAIRS = B // PAIR
    assert GROUPS_PER_BLOCK == X_SLOTS and B == P and S == HALF and D == H == 2 * P and SPREAD * ROWS == S

    x_rows = x.rearrange("b (a r) d -> (b a) (r d)", r=ROWS)
    out_rows = out.rearrange("b s h -> (b s) h")
    weight_loads = weights.rearrange("c (k p) h -> c p k h", p=P)

    with ExitStack() as ctx:
        def sb(name, shape, dt=F32):
            return ctx.enter_context(nc.sbuf_tensor(name, shape, dt))

        def sem(name):
            return ctx.enter_context(nc.semaphore(name))

        w_all = sb("w_all", [P, C, K, H])
        w_slot = sb("w_slot", [P, WEIGHT_SLOTS, K, H])
        x_nat = sb("x_nat", [P, X_SLOTS, ROWS, D])
        xT = sb("xT", [P, XT_SLOTS, K, GROUP, S])
        xbT = sb("xbT", [P, XT_SLOTS, K, GROUP, S])
        out_sb = sb("out_sb", [P, OUT_SLOTS, PAIR, H])

        ident = sb("ident", [P, P])
        zeros = sb("zeros", [P, P])
        iota_free = sb("iota_free", [P, P])
        iota_part = sb("iota_part", [P, 1])
        iota_part_i = sb("iota_part_i", [P, 1], I32)
        spread_i = sb("spread_i", [P, 1], I32)
        half_i = sb("half_i", [P, 1], I32)
        row_in_spread = sb("row_in_spread", [P, 1])
        row_in_half = sb("row_in_half", [P, 1])
        x_row0 = sb("x_row0", [P, 1])
        out_row0 = sb("out_row0", [P, 1])
        cat_row_i = sb("cat_row_i", [P, B], I32)
        cat_col_i = sb("cat_col_i", [P, 1], I32)
        cat_col = sb("cat_col", [P, 1])
        key_row = sb("key_row", [P, B])
        key_col = sb("key_col", [P, 1])
        smaller = sb("smaller", [P, B])
        rank = sb("rank", [P, 1])
        at_position = sb("at_position", [P, B])
        in_category = sb("in_category", [P, C])
        place_of_partition = sb("place_of_partition", [P, GROUP, SPREAD])
        place_fraction = sb("place_fraction", [P, GROUP, SPREAD])
        group_starts = sb("group_starts", [P, GROUPS])
        started = sb("started", [P, GROUPS - 1])
        group_of = sb("group_of", [P, 1])
        rank_in_groups = sb("rank_in_groups", [P, 1])
        which_group = sb("which_group", [P, GROUPS])
        place_in_pair = sb("place_in_pair", [P, PAIR])
        which_pair = sb("which_pair", [P, PAIRS])
        x_place = sb("x_place", [P, GROUP, SPREAD])
        out_row_of = sb("out_row_of", [P, PAIR, HALF])
        x_index = sb("x_index", [P, GROUPS], I32)
        out_index = sb("out_index", [P, PAIRS], I32)
        cat_sorted = sb("cat_sorted", [1, B], I32)
        samples_of = sb("samples_of", [1, C], I32)
        ones = sb("ones", [P, 1])
        sample_sorted = sb("sample_sorted", [1, B], I32)
        sorted_in_category = sb("sorted_in_category", [C, B])
        bias_nat = sb("bias_nat", [C, H])
        bias_sorted = sb("bias_sorted", [P, K, B])

        xt_ps = [[ctx.enter_context(nc.psum_tensor(f"xt_ps{g}{k}", [P, ROWS, GROUP, SPREAD], F32))
                  for k in range(K)] for g in range(XT_SLOTS)]
        mm_ps = [ctx.enter_context(nc.psum_tensor(f"mm_ps{r}", [P, PAIR, H], F32))
                 for r in range(BANKS)]
        last_pairs_ps = [ps for n in range(GROUP // QUAD) for ps in (
            mm_ps[(QUADS - GROUP // QUAD + n) % BANKS][:, 0, :],
            xt_ps[GROUPS % XT_SLOTS][n][:, :, :, :].rearrange("p r j a -> p (r j a)")[:, 0:H])]
        x_index_ps = mm_ps[0][:, 0, 0:GROUPS]
        out_index_ps = mm_ps[0][:, 1, 0:PAIRS]
        cat_sorted_ps = mm_ps[1][0:1, 0, 0:B]
        sample_sorted_ps = mm_ps[1][0:1, 1, 0:B]
        samples_of_ps = mm_ps[2][0:1, 1, 0:C]
        sorted_ps = mm_ps[2][0:C, 0, 0:B]
        bias_ps = mm_ps[3][:, 0, :].rearrange("p (k b) -> p k b", k=K)

        cats_loaded = sem("cats_loaded")
        bias_loaded = sem("bias_loaded")
        const_step = sem("const_step")
        consts_ready = sem("consts_ready")
        plan_step = sem("plan_step")
        plan_products = sem("plan_products")
        plan_read = sem("plan_read")
        w_loaded = [sem(f"w_loaded{n}") for n in range(LOADS_IN_FLIGHT)]
        w_loads_done = sem("w_loads_done")
        x_loaded = [sem(f"x_loaded{n}") for n in range(X_SLOTS)]
        halves_transposed = sem("halves_transposed")
        xT_ready = sem("xT_ready")
        xbT_ready = sem("xbT_ready")
        even_weights_ready = sem("even_weights_ready")
        odd_weights_ready = sem("odd_weights_ready")
        pairs_done = sem("pairs_done")
        quads_copied = sem("quads_copied")
        stored = [sem(f"stored{n}") for n in range(OUT_SLOTS)]
        odd_stored = sem("odd_stored")

        shared = range(QUADS - SHARED_FROM, QUADS - SHARED_TO)
        assert len(shared) < OUT_SLOTS and SHARED_FROM <= OUT_SLOTS
        last_group = QUADS - GROUP // QUAD

        def copies_until(q, p):
            return q + 1 if q < last_group else last_group + PAIR * (q - last_group) + p + 1

        def scatters_until(q):
            in_slot = range(q % OUT_SLOTS, q + 1, OUT_SLOTS)
            return sum(1 if n in shared else PAIR for n in in_slot)

        block = ctx.enter_context(nc.Block())

        @block.sync
        def _(sp):
            sp.dma_start(cat_row_i[:, :], cat.partition_broadcast(P)).then_inc(cats_loaded, 16)
            sp.dma_start(cat_col_i[:, :], cat.rearrange("(b a) -> b a", a=1)).then_inc(cats_loaded, 16)

            def load(c, slot, **when):
                sp.dma_start(w_all[:, bass.ds(c, 1), :, :].rearrange("p c k h -> p (c k) h"),
                             weight_loads[bass.ds(c, 1)].rearrange("c p k h -> p (c k) h"), **when
                             ).then_inc(w_loaded[slot], 16)

            def loaded(turn, slot):
                sp.wait_ge(w_loaded[slot], 16 * (turn + 1))
                sp.sem_inc(w_loads_done, 1)

            for slot in range(LOADS_IN_FLIGHT):
                load(slot, slot)
                if slot == 0:
                    sp.dma_start(bias_nat[:, :], bias).then_inc(bias_loaded, 16)
            for slot in range(UNCHECKED_LOADS - LOADS_IN_FLIGHT):
                loaded(0, slot)
                load(LOADS_IN_FLIGHT + slot, slot)

            def load_if_needed(turn, slot):
                c = turn * LOADS_IN_FLIGHT + slot
                samples = sp.value_load(samples_of[0:1, bass.ds(c, 1)], min_val=0, max_val=B)
                loaded(turn - 1, slot)
                load(c, slot, cond=samples > 0)

            sp.wait_ge(plan_read, 2)
            for slot in range(UNCHECKED_LOADS - LOADS_IN_FLIGHT, LOADS_IN_FLIGHT):
                load_if_needed(1, slot)
            with sp.Fori(2, C // LOADS_IN_FLIGHT) as turn:
                for slot in range(LOADS_IN_FLIGHT):
                    load_if_needed(turn, slot)
            for slot in range(LOADS_IN_FLIGHT):
                loaded(C // LOADS_IN_FLIGHT - 1, slot)

            sp.wait_ge(plan_read, 5)
            for q in shared:
                t = PAIR * q + 1
                samples = [sp.value_load(sample_sorted[0:1, PAIR * t + half:PAIR * t + half + 1],
                                         min_val=0, max_val=B - 1) for half in range(PAIR)]
                sp.wait_ge(quads_copied, copies_until(q, 1))
                for half in range(PAIR):
                    sp.dma_start(out[bass.ds(samples[half], 1), :, :].rearrange("b s h -> (b s) h"),
                                 out_sb[HALF * half:HALF * (half + 1), q % OUT_SLOTS, 1, :]
                                 ).then_inc(odd_stored, 16)
            sp.wait_ge(odd_stored, 16 * PAIR * len(shared))

        @block.gpsimd
        def _(pool):
            pool.iota(iota_free[:, :], [[1, P]], base=0, channel_multiplier=0,
                      allow_small_or_imprecise_dtypes=True).then_inc(consts_ready, 1)
            pool.iota(iota_part[:, :], [[0, 1]], base=0, channel_multiplier=1,
                      allow_small_or_imprecise_dtypes=True).then_inc(consts_ready, 1)
            pool.iota(iota_part_i[:, :], [[0, 1]], base=0, channel_multiplier=1).then_inc(consts_ready, 1)
            pool.iota(place_of_partition[:, :, :], [[1, GROUP], [0, SPREAD]], base=0, channel_multiplier=0,
                      allow_small_or_imprecise_dtypes=True).then_inc(consts_ready, 1)
            pool.iota(group_starts[:, :], [[GROUP, GROUPS]], base=0, channel_multiplier=0,
                      allow_small_or_imprecise_dtypes=True).then_inc(consts_ready, 1)
            pool.memset(ones[:, :], 1.0).then_inc(consts_ready, 1)
            pool.memset(zeros[:, :], 0.0).then_inc(const_step, 1)
            pool.wait_ge(const_step, 1)
            pool.affine_select(out=ident[:, :], in_=zeros[:, :], compare_op=ALU.not_equal, fill=1.0, base=0,
                               pattern=[[-1, P]], channel_multiplier=1).then_inc(consts_ready, 1)

            def gather(g):
                if g >= X_SLOTS:
                    pool.wait_ge(halves_transposed, K * (g - X_SLOTS + 1))
                pool.indirect_dma_start(
                    x_nat[:, g % X_SLOTS, :, :].rearrange("p r d -> p (r d)"), None, x_rows,
                    bass.IndirectOffsetOnAxis(ap=x_index[:, g:g + 1], axis=0)
                ).then_inc(x_loaded[g % X_SLOTS], 16)

            def scatter(q):
                for p in range(1 if q in shared else PAIR):
                    t = PAIR * q + p
                    pool.wait_ge(quads_copied, copies_until(q, p))
                    pool.indirect_dma_start(
                        out_rows, bass.IndirectOffsetOnAxis(ap=out_index[:, t:t + 1], axis=0),
                        out_sb[:, q % OUT_SLOTS, p, :], None).then_inc(stored[q % OUT_SLOTS], 16)

            pool.wait_ge(plan_read, 1)
            for g in range(X_AHEAD):
                gather(g)
            pool.wait_ge(plan_read, 3)
            for q in range(QUADS):
                g = q * QUAD // GROUP + X_AHEAD
                if q * QUAD % GROUP == 0 and g < GROUPS:
                    gather(g)
                if q >= 1:
                    scatter(q - 1)
            scatter(QUADS - 1)
            for q in range(QUADS - OUT_SLOTS, QUADS):
                pool.wait_ge(stored[q % OUT_SLOTS], 16 * scatters_until(q))

        def copy_weights(eng, copy, t, r, p, half, ready):
            j = PAIR * t + half
            slot = (QUAD * ((r + 1) % QUADS_PER_BLOCK) + PAIR * p + half) % WEIGHT_SLOTS
            c = eng.value_load(cat_sorted[0:1, bass.ds(j, 1)], min_val=0, max_val=C - 1)
            eng.wait_ge(w_loads_done, c + 1)
            copy(w_slot[:, slot, :, :].rearrange("p k h -> p (k h)"),
                 w_all[:, bass.ds(c, 1), :, :].rearrange("p c k h -> p (c k h)")).then_inc(ready, 1)

        @block.scalar
        def _(act):
            def x_half(g, slot, k):
                act.wait_ge(halves_transposed, K * g + k + 1)
                nc.scalar.copy(xT[:, slot, k].rearrange("p j (a r) -> p r j a", r=ROWS),
                               xt_ps[slot][k][:, :, :, :]).then_inc(xT_ready, 1)

            def quad(it, r):
                q, g, k = QUADS_PER_BLOCK * it + r, GROUPS_PER_BLOCK * it + r // K, r % K
                static = isinstance(it, int)
                if not static or g + 1 < GROUPS:
                    if not static or g >= 1:
                        act.wait_ge(pairs_done, GROUP // PAIR * g)
                    x_half(g + 1, (r // K + 1) % XT_SLOTS, k)
                if not static or q + 1 < QUADS:
                    weights_of_next(it, r, q)

            def weights_of_next(it, r, q):
                for p in range(PAIR):
                    t = PAIR * (q + 1) + p
                    if not isinstance(it, int) or t >= WEIGHT_SLOTS // PAIR:
                        act.wait_ge(pairs_done, t - WEIGHT_SLOTS // PAIR + 1)
                    copy_weights(act, nc.scalar.copy, t, r, p, 1, odd_weights_ready)

            for k in range(K):
                x_half(0, 0, k)
            act.wait_ge(plan_read, 5)
            weights_of_next(0, QUADS_PER_BLOCK - 1, -1)
            for r in range(QUADS_PER_BLOCK):
                quad(0, r)
            with act.Fori(1, BLOCKS - 1) as it:
                for r in range(QUADS_PER_BLOCK):
                    quad(it, r)
            for r in range(QUADS_PER_BLOCK):
                quad(BLOCKS - 1, r)

        @block.vector
        def _(dve):
            steps = [0]

            def step(instruction):
                steps[0] += 1
                instruction.then_inc(plan_step, 1)
                dve.wait_ge(plan_step, steps[0])

            V = nc.vector
            dve.wait_ge(consts_ready, 5)
            V.tensor_single_scalar(spread_i[:, :], iota_part_i[:, :], SPREAD - 1, ALU.bitwise_and
                                   ).then_inc(plan_step, 1)
            V.tensor_single_scalar(half_i[:, :], iota_part_i[:, :], HALF - 1, ALU.bitwise_and
                                   ).then_inc(plan_step, 1)
            V.tensor_scalar(place_fraction[:, :, :], place_of_partition[:, :, :], 1.0 / GROUP, None, ALU.mult
                            ).then_inc(plan_step, 1)
            V.tensor_scalar(x_row0[:, :], iota_part[:, :], float(SPREAD), None, ALU.mult).then_inc(plan_step, 1)
            V.tensor_scalar(out_row0[:, :], iota_part[:, :], float(S), None, ALU.mult).then_inc(plan_step, 1)
            steps[0] += 5
            dve.wait_ge(plan_step, steps[0])
            V.tensor_copy(row_in_spread[:, :], spread_i[:, :]).then_inc(plan_step, 1)
            V.tensor_copy(row_in_half[:, :], half_i[:, :]).then_inc(plan_step, 1)
            steps[0] += 2
            dve.wait_ge(cats_loaded, 32)
            V.tensor_copy(cat_col[:, :], cat_col_i[:, :]).then_inc(plan_step, 1)
            steps[0] += 1
            V.scalar_tensor_tensor(out=key_row[:, :], in0=cat_row_i[:, :], scalar=float(B), in1=iota_free[:, :],
                                   op0=ALU.mult, op1=ALU.add).then_inc(plan_step, 1)
            steps[0] += 1
            step(V.scalar_tensor_tensor(out=key_col[:, :], in0=cat_col_i[:, :], scalar=float(B),
                                        in1=iota_part[:, :], op0=ALU.mult, op1=ALU.add))
            step(V.tensor_scalar(smaller[:, :], key_row[:, :], key_col[:, 0:1], 0.0, ALU.is_lt, ALU.add,
                                 accum_out=rank[:, 0:1]))
            V.tensor_scalar(started[:, :], group_starts[:, 1:GROUPS], rank[:, 0:1], 0.0, ALU.is_le, ALU.add,
                            accum_out=group_of[:, 0:1]).then_inc(plan_step, 1)
            V.tensor_scalar(rank_in_groups[:, :], rank[:, :], 1.0 / GROUP, None, ALU.mult
                            ).then_inc(plan_step, 1)
            steps[0] += 2
            dve.wait_ge(plan_step, steps[0])
            V.tensor_scalar(x_place[:, :, :], place_fraction[:, :, :], group_of[:, 0:1],
                            rank_in_groups[:, 0:1], ALU.add, ALU.is_equal).then_inc(plan_step, 1)
            V.tensor_scalar(which_group[:, :], iota_free[:, 0:GROUPS], group_of[:, 0:1], x_row0[:, 0:1],
                            ALU.is_equal, ALU.mult).then_inc(plan_step, 1)
            steps[0] += 2
            X_PLAN = steps[0]
            step(V.tensor_scalar(at_position[:, :], iota_free[:, :], rank[:, 0:1], None, ALU.is_equal))
            V.tensor_scalar(in_category[:, :], iota_free[:, 0:C], cat_col[:, 0:1], None, ALU.is_equal
                            ).then_inc(plan_step, 1)
            V.tensor_reduce(place_in_pair[:, :], at_position[:, :].rearrange("p (t j) -> p j t", j=PAIR),
                            AX_X, ALU.add).then_inc(plan_step, 1)
            steps[0] += 2
            step(V.tensor_reduce(which_pair[:, :], at_position[:, :].rearrange("p (t j) -> p t j", j=PAIR),
                                 AX_X, ALU.add))
            assert (X_PLAN, steps[0]) == (PLAN_STEPS["x"], PLAN_STEPS["categories"])
            dve.wait_ge(plan_products, 1)
            V.tensor_scalar(x_index[:, :], x_index_ps, row_in_spread[:, 0:1], None, ALU.add
                            ).then_inc(plan_read, 1)
            step(V.tensor_scalar(out_row_of[:, :, :],
                                 place_in_pair[:, :].unsqueeze(2).broadcast_to([P, PAIR, HALF]),
                                 out_row0[:, 0:1], None, ALU.mult))
            assert steps[0] == PLAN_STEPS["out"]
            dve.wait_ge(plan_products, 5)
            V.tensor_copy(samples_of[:, :], samples_of_ps).then_inc(plan_read, 1)
            step(V.tensor_copy(sorted_in_category[:, :], sorted_ps))
            assert steps[0] == PLAN_STEPS["sorted"]
            dve.wait_ge(plan_products, 6)
            V.tensor_scalar(out_index[:, :], out_index_ps, row_in_half[:, 0:1], None, ALU.add
                            ).then_inc(plan_read, 1)
            V.tensor_copy(sample_sorted[:, :], sample_sorted_ps).then_inc(plan_read, 1)
            V.tensor_copy(cat_sorted[:, :], cat_sorted_ps).then_inc(plan_read, 1)
            dve.wait_ge(plan_products, 7)
            V.tensor_copy(bias_sorted[:, :, :], bias_ps).then_inc(plan_read, 1)

            def xb_half(g, slot, k):
                dve.wait_ge(xT_ready, K * g + k + 1)
                V.tensor_tensor(
                    xbT[:, slot, k].rearrange("p j (a r) -> p r j a", r=ROWS), xt_ps[slot][k][:, :, :, :],
                    bias_sorted[:, k, bass.ds(GROUP * g, GROUP)].unsqueeze(1).unsqueeze(3).broadcast_to(
                        [P, ROWS, GROUP, SPREAD]), ALU.add).then_inc(xbT_ready, 1)

            def copy_out(slot, q):
                dve.wait_ge(pairs_done, PAIR * (q + 1))
                V.tensor_copy(out_sb[:, slot, :, :], mm_ps[slot][:, :, :]).then_inc(quads_copied, 1)

            def slot_is_free(q):
                dve.wait_ge(stored[q % OUT_SLOTS], 16 * scatters_until(q - OUT_SLOTS))

            def copy_out_pairs(q):
                for p in range(PAIR):
                    t = PAIR * q + p
                    dve.wait_ge(pairs_done, t + 1)
                    V.tensor_copy(out_sb[:, q % OUT_SLOTS, p, :], last_pairs_ps[t - PAIRS + GROUP // PAIR]
                                  ).then_inc(quads_copied, 1)

            def quad(it, r):
                q, g, k = QUADS_PER_BLOCK * it + r, GROUPS_PER_BLOCK * it + r // K, r % K
                static = isinstance(it, int)
                if not static or g + 1 < GROUPS:
                    if not static or g >= 1:
                        dve.wait_ge(pairs_done, GROUP // PAIR * g)
                    xb_half(g + 1, (r // K + 1) % XT_SLOTS, k)
                if not static or q + 1 < QUADS:
                    weights_of_next(it, r, q)
                if not static or q >= 1:
                    turn = QUADS_PER_BLOCK // OUT_SLOTS * it + (r - 1) // OUT_SLOTS
                    if not static:
                        dve.wait_ge(stored[(r - 1) % OUT_SLOTS], 16 * PAIR * turn)
                    elif turn >= 1:
                        slot_is_free(q - 1)
                    if not static or q - 1 < QUADS - GROUP // QUAD:
                        copy_out((r - 1) % OUT_SLOTS, q - 1)
                    else:
                        copy_out_pairs(q - 1)

            def weights_of_next(it, r, q):
                for p in range(PAIR):
                    t = PAIR * (q + 1) + p
                    if not isinstance(it, int) or t >= WEIGHT_SLOTS // PAIR:
                        dve.wait_ge(pairs_done, t - WEIGHT_SLOTS // PAIR + 1)
                    copy_weights(dve, V.tensor_copy, t, r, p, 0, even_weights_ready)

            dve.wait_ge(plan_read, 6)
            for k in range(K):
                xb_half(0, 0, k)
            weights_of_next(0, QUADS_PER_BLOCK - 1, -1)
            for r in range(QUADS_PER_BLOCK):
                quad(0, r)
            with dve.Fori(1, BLOCKS - 1) as it:
                for r in range(QUADS_PER_BLOCK):
                    quad(it, r)
            for r in range(QUADS_PER_BLOCK):
                quad(BLOCKS - 1, r)
            slot_is_free(QUADS - 1)
            copy_out_pairs(QUADS - 1)

        @block.tensor
        def _(pe):
            T = nc.tensor

            def warm_up(times):
                for _ in range(times):
                    T.transpose(xt_ps[1][0][:, 0, :, :].rearrange("p j a -> p (j a)"), ident[:, :], ident[:, :])

            pe.wait_ge(plan_step, PLAN_STEPS["x"])
            T.matmul(x_index_ps, x_place[:, :, :].rearrange("p j a -> p (j a)"), which_group[:, :],
                     start=True, stop=True).then_inc(plan_products, 1)
            pe.wait_ge(plan_step, PLAN_STEPS["categories"])
            pe.wait_ge(consts_ready, 7)
            T.matmul(samples_of_ps, ones[:, :], in_category[:, :], start=True, stop=True
                     ).then_inc(plan_products, 1)
            T.matmul(cat_sorted_ps, cat_col[:, :], at_position[:, :], start=True, stop=True
                     ).then_inc(plan_products, 1)
            T.matmul(sample_sorted_ps, iota_part[:, :], at_position[:, :], start=True, stop=True
                     ).then_inc(plan_products, 1)
            T.matmul(sorted_ps, in_category[:, :], at_position[:, :], start=True, stop=True
                     ).then_inc(plan_products, 1)
            pe.wait_ge(plan_step, PLAN_STEPS["out"])
            pe.wait_ge(plan_read, 1)
            T.matmul(out_index_ps, out_row_of[:, :, :].rearrange("p j a -> p (j a)"), which_pair[:, :],
                     start=True, stop=True).then_inc(plan_products, 1)
            warm_up(WARM_UP[0])
            pe.wait_ge(plan_step, PLAN_STEPS["sorted"])
            pe.wait_ge(bias_loaded, 16)
            for k in range(K):
                last = T.matmul(bias_ps[:, k, :], bias_nat[:, k * P:(k + 1) * P], sorted_in_category[:, :],
                                start=True, stop=True)
            last.then_inc(plan_products, 1)

            def transpose_half(x_slot, slot, k):
                for r in range(ROWS):
                    last = T.transpose(xt_ps[slot][k][:, r, :, :].rearrange("p j a -> p (j a)"),
                                       x_nat[:, x_slot, r, k * P:(k + 1) * P], ident[:, :])
                last.then_inc(halves_transposed, 1)

            def group(it, r):
                g = GROUPS_PER_BLOCK * it + r
                static = isinstance(it, int)

                def sums(quad, p):
                    if static and g == GROUPS - 1:
                        return last_pairs_ps[PAIR * quad + p]
                    return mm_ps[(GROUP // QUAD * r + quad) % BANKS][:, p, :]

                x_slot, slot, next_slot = (r + 1) % X_SLOTS, r % XT_SLOTS, (r + 1) % XT_SLOTS
                if not static or g + 1 < GROUPS:
                    pe.wait_ge(x_loaded[x_slot], 16 * (it + (r + 1) // X_SLOTS + 1))
                    for k in range(K):
                        if not static or g + 1 >= XT_SLOTS:
                            pe.wait_ge(xbT_ready, K * (g + 1 - XT_SLOTS) + k + 1)
                        transpose_half(x_slot, next_slot, k)
                pe.wait_ge(xbT_ready, K * g + K)
                for quad in range(GROUP // QUAD):
                    q = GROUP // QUAD * g + quad
                    if not static or q >= BANKS:
                        pe.wait_ge(quads_copied, q - BANKS + 1)
                    for p in range(PAIR):
                        j = QUAD * quad + PAIR * p
                        to = sums(quad, p)
                        for k in range(K):
                            T.matmul(to[:, k * P:(k + 1) * P],
                                     xbT[:, slot, k, j:j + PAIR, :].rearrange("p j s -> p (j s)"), ident[:, :],
                                     start=(k == 0 and (p == 0 or (static and g == GROUPS - 1))), stop=False, is_transpose=True,
                                     skip_group_check=True)
                for pair in range(GROUP // PAIR):
                    t = GROUP // PAIR * g + pair
                    to = sums(pair // PAIR, pair % PAIR)
                    pe.wait_ge(even_weights_ready, t + 1)
                    pe.wait_ge(odd_weights_ready, t + 1)
                    for k in range(K):
                        for half in range(PAIR):
                            j = PAIR * pair + half
                            last = T.matmul(to[HALF * half:HALF * (half + 1), :],
                                            xT[:, slot, k, j, :], w_slot[:, (GROUP * r + j) % WEIGHT_SLOTS, k, :],
                                            start=False, stop=(k == K - 1), skip_group_check=True)
                    last.then_inc(pairs_done, 1)

            warm_up(WARM_UP[1])
            pe.wait_ge(x_loaded[0], 16)
            for k in range(K):
                transpose_half(0, 0, k)
            pe.wait_ge(plan_read, 6)
            for r in range(GROUPS_PER_BLOCK):
                group(0, r)
            with pe.Fori(1, BLOCKS - 1) as it:
                for r in range(GROUPS_PER_BLOCK):
                    group(it, r)
            for r in range(GROUPS_PER_BLOCK):
                group(BLOCKS - 1, r)


_INS = ["x", "itok_B_0_63", "L0_cond_W", "L0_cond_b"]


def kernel(**inputs):
    import numpy as np
    import concourse.bacc as bacc
    from concourse.bass_utils import run_bass_kernel_spmd

    nc = bacc.Bacc("TRN2", target_bir_lowering=False, num_devices=1)
    arrays, args = {}, []
    for name in _INS:
        a = np.ascontiguousarray(inputs[name])
        arrays[f"in_{name}"] = a
        args.append(nc.dram_tensor(f"in_{name}", a.shape, mybir.dt.from_np(a.dtype), kind="ExternalInput").ap())
    shape = inputs["x"].shape
    out = nc.dram_tensor("out", shape, mybir.dt.float32, kind="ExternalOutput").ap()
    build_cond_residual(nc, *args, out)
    result = run_bass_kernel_spmd(nc, [arrays], core_ids=[0])
    return result.results[0]["out"]
```
